# Optimizing a Trainium2 kernel written in Bass

```python
import numpy as np
import jax
import jax.numpy as jnp

def _softmax(x, axis=-1):
    return jax.nn.softmax(x, axis=axis)
def _gelu(x):
    return jax.nn.gelu(x, approximate=True)
def _silu(x):
    return jax.nn.silu(x)
def _sigmoid(x):
    return jax.nn.sigmoid(x)
def _layernorm(x, axis=-1, eps=1e-5):
    m = jnp.mean(x, axis=axis, keepdims=True)
    v = jnp.var(x, axis=axis, keepdims=True)
    return (x - m) / jnp.sqrt(v + eps)
def _scatter_add(tgt, idx, src, axis=0):
    return tgt.at[idx].add(src)
def _segment_sum(src, seg, n):
    return jax.ops.segment_sum(src, seg, n)

kernel_name = 'mk_rec_standalone_d1_rec_907489'

def setup_inputs(seed: int = 0):
    np.random.seed(seed)
    _w = jnp.asarray
    def _rec_inputs():
        import jax
        import jax.numpy as jnp
        _rk = jax.random.key(seed)
        r_x = jnp.stack([jax.random.randint(jax.random.fold_in(jax.random.fold_in(_rk, 1), 0), (4096,), 17, 99919, jnp.int32), jax.random.randint(jax.random.fold_in(jax.random.fold_in(_rk, 1), 1), (4096,), 33, 99987, jnp.int32), jax.random.randint(jax.random.fold_in(jax.random.fold_in(_rk, 1), 2), (4096,), 29, 99990, jnp.int32), jax.random.randint(jax.random.fold_in(jax.random.fold_in(_rk, 1), 3), (4096,), 6, 99982, jnp.int32), jax.random.randint(jax.random.fold_in(jax.random.fold_in(_rk, 1), 4), (4096,), 68, 99886, jnp.int32), jax.random.randint(jax.random.fold_in(jax.random.fold_in(_rk, 1), 5), (4096,), 19, 99949, jnp.int32), jax.random.randint(jax.random.fold_in(jax.random.fold_in(_rk, 1), 6), (4096,), 98, 99935, jnp.int32), jax.random.randint(jax.random.fold_in(jax.random.fold_in(_rk, 1), 7), (4096,), 10, 99952, jnp.int32), jax.random.randint(jax.random.fold_in(jax.random.fold_in(_rk, 1), 8), (4096,), 53, 99966, jnp.int32), jax.random.randint(jax.random.fold_in(jax.random.fold_in(_rk, 1), 9), (4096,), 13, 99957, jnp.int32), jax.random.randint(jax.random.fold_in(jax.random.fold_in(_rk, 1), 10), (4096,), 81, 99987, jnp.int32), jax.random.randint(jax.random.fold_in(jax.random.fold_in(_rk, 1), 11), (4096,), 1, 99952, jnp.int32), jax.random.randint(jax.random.fold_in(jax.random.fold_in(_rk, 1), 12), (4096,), 22, 99962, jnp.int32), jax.random.randint(jax.random.fold_in(jax.random.fold_in(_rk, 1), 13), (4096,), 17, 99980, jnp.int32), jax.random.randint(jax.random.fold_in(jax.random.fold_in(_rk, 1), 14), (4096,), 46, 99967, jnp.int32), jax.random.randint(jax.random.fold_in(jax.random.fold_in(_rk, 1), 15), (4096,), 83, 99942, jnp.int32), jax.random.randint(jax.random.fold_in(jax.random.fold_in(_rk, 1), 16), (4096,), 1, 99971, jnp.int32), jax.random.randint(jax.random.fold_in(jax.random.fold_in(_rk, 1), 17), (4096,), 11, 99986, jnp.int32), jax.random.randint(jax.random.fold_in(jax.random.fold_in(_rk, 1), 18), (4096,), 86, 99996, jnp.int32), jax.random.randint(jax.random.fold_in(jax.random.fold_in(_rk, 1), 19), (4096,), 18, 99978, jnp.int32), jax.random.randint(jax.random.fold_in(jax.random.fold_in(_rk, 1), 20), (4096,), 35, 99975, jnp.int32), jax.random.randint(jax.random.fold_in(jax.random.fold_in(_rk, 1), 21), (4096,), 55, 99946, jnp.int32), jax.random.randint(jax.random.fold_in(jax.random.fold_in(_rk, 1), 22), (4096,), 92, 99926, jnp.int32), jax.random.randint(jax.random.fold_in(jax.random.fold_in(_rk, 1), 23), (4096,), 96, 99987, jnp.int32), jax.random.randint(jax.random.fold_in(jax.random.fold_in(_rk, 1), 24), (4096,), 5, 99965, jnp.int32), jax.random.randint(jax.random.fold_in(jax.random.fold_in(_rk, 1), 25), (4096,), 36, 99942, jnp.int32), jax.random.randint(jax.random.fold_in(jax.random.fold_in(_rk, 1), 26), (4096,), 142, 99939, jnp.int32), jax.random.randint(jax.random.fold_in(jax.random.fold_in(_rk, 1), 27), (4096,), 20, 99962, jnp.int32), jax.random.randint(jax.random.fold_in(jax.random.fold_in(_rk, 1), 28), (4096,), 3, 99951, jnp.int32), jax.random.randint(jax.random.fold_in(jax.random.fold_in(_rk, 1), 29), (4096,), 15, 99942, jnp.int32), jax.random.randint(jax.random.fold_in(jax.random.fold_in(_rk, 1), 30), (4096,), 39, 99917, jnp.int32), jax.random.randint(jax.random.fold_in(jax.random.fold_in(_rk, 1), 31), (4096,), 14, 99964, jnp.int32), jax.random.randint(jax.random.fold_in(jax.random.fold_in(_rk, 1), 32), (4096,), 39, 99990, jnp.int32), jax.random.randint(jax.random.fold_in(jax.random.fold_in(_rk, 1), 33), (4096,), 229, 99942, jnp.int32), jax.random.randint(jax.random.fold_in(jax.random.fold_in(_rk, 1), 34), (4096,), 52, 99945, jnp.int32), jax.random.randint(jax.random.fold_in(jax.random.fold_in(_rk, 1), 35), (4096,), 60, 99985, jnp.int32), jax.random.randint(jax.random.fold_in(jax.random.fold_in(_rk, 1), 36), (4096,), 153, 99923, jnp.int32), jax.random.randint(jax.random.fold_in(jax.random.fold_in(_rk, 1), 37), (4096,), 15, 99906, jnp.int32), jax.random.randint(jax.random.fold_in(jax.random.fold_in(_rk, 1), 38), (4096,), 44, 99993, jnp.int32), jax.random.randint(jax.random.fold_in(jax.random.fold_in(_rk, 1), 39), (4096,), 14, 99904, jnp.int32)], axis=1)
        return r_x
    r_x = _rec_inputs()
    def _L0_rec_setup():
        import jax, jax.numpy as jnp
        import numpy as np
        N_VOCAB = 100000
        N_FIELDS = 40
        K = 64
        ATTN = 64
        BATCH = 2048
        key = jax.random.key(seed)
        ks = jax.random.split(key, 9)
        x = jax.random.randint(ks[0], (BATCH, N_FIELDS), 0, N_VOCAB)
        lin_table = jax.random.normal(ks[1], (N_VOCAB, 1), dtype=jnp.float32) * 0.01
        V_table = jax.random.normal(ks[2], (N_VOCAB, K), dtype=jnp.float32) * 0.01
        W1 = jax.random.normal(ks[3], (K, ATTN), dtype=jnp.float32) * (1.0 / np.sqrt(K))
        b1 = jnp.zeros((ATTN,), dtype=jnp.float32)
        W2 = jax.random.normal(ks[4], (ATTN, 1), dtype=jnp.float32) * (1.0 / np.sqrt(ATTN))
        b2 = jnp.zeros((1,), dtype=jnp.float32)
        Wf = jax.random.normal(ks[5], (K, 1), dtype=jnp.float32) * (1.0 / np.sqrt(K))
        bf = jnp.zeros((1,), dtype=jnp.float32)
        return {'x': x, 'lin_table': lin_table, 'V_table': V_table, 'W1': W1, 'b1': b1, 'W2': W2, 'b2': b2, 'Wf': Wf, 'bf': bf}
    _L0_rec_all = _L0_rec_setup()
    _L0_rec_in = {k: v for k, v in _L0_rec_all.items() if k in ('lin_table', 'V_table', 'W1', 'b1', 'W2', 'b2', 'Wf', 'bf', )}
    del _L0_rec_all

    return {
        "r_x": r_x,
        "L0_rec_lin_table": _L0_rec_in["lin_table"],
        "L0_rec_V_table": _L0_rec_in["V_table"],
        "L0_rec_W1": _L0_rec_in["W1"],
        "L0_rec_b1": _L0_rec_in["b1"],
        "L0_rec_W2": _L0_rec_in["W2"],
        "L0_rec_b2": _L0_rec_in["b2"],
        "L0_rec_Wf": _L0_rec_in["Wf"],
        "L0_rec_bf": _L0_rec_in["bf"],
    }

def reference(r_x, L0_rec_lin_table, L0_rec_V_table, L0_rec_W1, L0_rec_b1, L0_rec_W2, L0_rec_b2, L0_rec_Wf, L0_rec_bf):
    import jax
    import jax.numpy as jnp
    def _L0_rec_ref(x, lin_table, V_table, W1, b1, W2, b2, Wf, bf):
        import jax, jax.numpy as jnp
        import numpy as np
        N_VOCAB = 100000
        N_FIELDS = 40
        K = 64
        ATTN = 64
        BATCH = 2048
        linear_part = jnp.sum(lin_table[x], axis=1)
        embd = V_table[x]
        pw = embd[:, :, None, :] * embd[:, None, :, :]
        h = jax.nn.relu(jnp.einsum('bijk,ka->bija', pw, W1) + b1)
        scores = jnp.einsum('bija,ao->bijo', h, W2) + b2
        probs = jax.nn.softmax(scores, axis=2)
        weighted = jnp.sum(probs * pw, axis=2)
        weighted_embd = jnp.sum(weighted, axis=1)
        interaction_part = weighted_embd @ Wf + bf
        return jax.nn.sigmoid(linear_part + interaction_part)[:, 0]

    y = _L0_rec_ref(r_x, L0_rec_lin_table, L0_rec_V_table, L0_rec_W1, L0_rec_b1, L0_rec_W2, L0_rec_b2, L0_rec_Wf, L0_rec_bf)
    return y


_drawn_inputs = setup_inputs


def setup_inputs(seed=0):
    import zlib

    import numpy as np

    out = dict(_drawn_inputs(seed))
    spreads = {'L0_rec_b1': (0.0, 0.8)}
    factors = {'L0_rec_V_table': 8.0, 'L0_rec_W1': 8.0, 'L0_rec_W2': 8.0, 'L0_rec_Wf': 8.0}
    for name, (base, spread) in spreads.items():
        noise = np.random.default_rng([zlib.crc32(name.encode()), seed]).standard_normal(out[name].shape)
        drawn = base * np.exp(spread * noise) if base else spread * noise
        out[name] = jnp.asarray(drawn.astype(out[name].dtype))
    for name, factor in factors.items():
        out[name] = (out[name] * factor).astype(out[name].dtype)
    return out
```

```python
from contextlib import ExitStack

import concourse.bass as bass
from concourse import mybir

ALU = mybir.AluOpType
ACT = mybir.ActivationFunctionType
F32 = mybir.dt.float32
I32 = mybir.dt.int32
AX_X = mybir.AxisListType.X

P = 128
BANK = 512
HALVES = 2


def attentional_fm(nc, x_idx, lin_first, lin_last, W1, b1, W2, b2, Wf, bf, out):
    G, _, FH = x_idx.shape
    F = FH // HALVES
    K = W1.shape[0]
    ROW = K + 1
    ND = F // 2 + 1
    NSK = F // 2 - 1
    FPC = BANK // P
    NQ = ND * F // FPC
    CPT = 5
    NT = NQ // CPT
    FPT = CPT * FPC
    TRING = 3
    HRING = 10
    STEP = 4
    NS = -(-NQ // STEP)
    SLOTS = 32 // HALVES
    NB = -(-NS // SLOTS)
    QPAD = NS * STEP
    NET = F // FPC
    FX = F + F // 2
    NDUP = (F // 2) // FPC
    NTAIL = 15
    SKEW = NSK * 2 * F
    assert 2 * K == P and NQ % CPT == 0 and NT % TRING == 0 and NQ % HRING == 0 and F % FPT == 0
    assert lin_first.shape[1] == lin_last.shape[1] == ROW

    with ExitStack() as ctx:
        def sb(name, shape, dt=F32):
            return ctx.enter_context(nc.sbuf_tensor(name, shape, dt))

        def sem(name):
            return ctx.enter_context(nc.semaphore(name))

        w1_diag = sb("w1_diag", [P, P])
        w2_slot = sb("w2_slot", [P, SLOTS * 32])
        wf_slot = sb("wf_slot", [P, SLOTS * 32])
        w2_col = sb("w2_col", [P, 1])
        wf_col = sb("wf_col", [P, 1])
        b1_col = sb("b1_col", [P, 1])
        b2_col = sb("b2_col", [P, 1])
        bf_col = sb("bf_col", [P, 1])
        ident = sb("ident", [P, P])
        idx = sb("idx", [P, FH], I32)
        gate = sb("gate", [P, 2])
        raw = sb("raw", [P, F, HALVES * ROW])
        et = sb("et", [P, 2, FX * P])
        prod = sb("prod", [P, TRING, FPT * P])
        hid = sb("hid", [P, HRING, BANK])
        stage = sb("stage", [P, 2, BANK])
        score = sb("score", [P, HALVES, QPAD * FPC])
        dot = sb("dot", [P, HALVES, QPAD * FPC])
        sc2 = sb("sc2", [P, HALVES, SKEW + F])
        mx = sb("mx", [P, 2, HALVES, F])
        mrow = sb("mrow", [P, HALVES, FX])
        pr1 = sb("pr1", [P, 2, HALVES, ND * F])
        pr2 = sb("pr2", [P, 2, HALVES, SKEW + F])
        zn = sb("zn", [P, 3, 2 * HALVES, F])
        rz = sb("rz", [P, HALVES, F])
        share = sb("share", [P, HALVES, F])
        inter = sb("inter", [P, G * HALVES])
        linear = sb("linear", [P, G * HALVES])
        logit = sb("logit", [P, 2, G * HALVES])
        prob = sb("prob", [P, G * HALVES])
        y_rows = sb("y_rows", [G * HALVES, P])
        ps = ctx.enter_context(nc.psum_tensor("ps", [P, 8, BANK], F32))
        Z, S, D, T_SG, T_ET = (0, 1), (2, 3), (4, 5), 6, 7

        w_zero = sem("w_zero")
        w_loaded = sem("w_loaded")
        w_ready = sem("w_ready")
        id_ready = sem("id_ready")
        gate_done = sem("gate_done")
        idx_loaded = sem("idx_loaded")
        gathered = sem("gathered")
        lin_done = sem("lin_done")
        et_done = sem("et_done")
        et_copied = sem("et_copied")
        prod_ready = sem("prod_ready")
        prod_used = sem("prod_used")
        z_done = sem("z_done")
        hid_ready = sem("hid_ready")
        block_done = sem("block_done")
        block_staged = sem("block_staged")
        sg_done = sem("sg_done")
        sg_copied = sem("sg_copied")
        tail = sem("tail")
        mrow_ext = sem("mrow_ext")
        share_done = sem("share_done")
        slot_zero = sem("slot_zero")
        exp_done = sem("exp_done")
        logit_ready = sem("logit_ready")
        prob_ready = sem("prob_ready")
        y_turned = sem("y_turned")
        y_ready = sem("y_ready")
        stored = sem("stored")

        block = ctx.enter_context(nc.Block())

        def wait(eng, s, value):
            if not isinstance(value, int) or value > 0:
                eng.wait_ge(s, value)

        def over_groups(eng, body):
            body(0, True, False)
            with eng.Fori(1, G - 1) as g:
                body(g, False, False)
            body(G - 1, False, True)

        def parity(g):
            return g % 2 if isinstance(g, int) else g & 1

        def skewable(t):
            return t[:, :, 0:SKEW].rearrange("p h (d x) -> p h d x", x=2 * F)

        def skewed(t):
            return t[:, :, F - 1:F - 1 + NSK * (2 * F - 1)].rearrange("p h (d x) -> p h x d", x=2 * F - 1)[:, :, 0:F, :]

        STAGE_AT = {SLOTS * (n + 1): n for n in range(NB - 1)}
        TURN_AT = {}
        for n in range(NB - 1):
            TURN_AT[SLOTS * (n + 1) + 2] = (n, 0)
            TURN_AT[SLOTS * (n + 1) + 3] = (n, 1)
        ET_AT = {36 + i: i for i in range(NET)}
        LIN_AT = 35
        LOAD_AT = 0
        EXP_AT = 10

        @block.sync
        def _(sp):
            sp.wait_ge(w_zero, 1)
            for h in range(HALVES):
                half = slice(K * h, K * (h + 1))
                sp.dma_start(w1_diag[half, half], W1).then_inc(w_loaded, 16)
                sp.dma_start(w2_col[half, :], W2).then_inc(w_loaded, 16)
                sp.dma_start(wf_col[half, :], Wf).then_inc(w_loaded, 16)
                sp.dma_start(b1_col[half, :], b1.rearrange("(a o) -> a o", o=1)).then_inc(w_loaded, 16)
            sp.dma_start(b2_col[:], b2.rearrange("(a o) -> a o", o=1).to_broadcast([P, 1])).then_inc(w_loaded, 16)
            sp.dma_start(bf_col[:], bf.rearrange("(a o) -> a o", o=1).to_broadcast([P, 1])).then_inc(w_loaded, 16)
            sp.dma_start(idx[:], x_idx[0]).then_inc(idx_loaded, 16)
            sp.wait_ge(y_ready, 1)
            sp.dma_start(out.rearrange("(c p) -> c p", p=P), y_rows[:]).then_inc(stored, 16)
            sp.wait_ge(stored, 16)

        @block.gpsimd
        def _(pool):
            nc.gpsimd.memset(gate[:], 0.0).then_inc(gate_done, 1)
            pool.wait_ge(gate_done, 1)
            nc.gpsimd.memset(w1_diag[:], 0.0).then_inc(w_zero, 1)


            def gather(g):
                pool.wait_ge(idx_loaded, g * 16 + 16)
                pool.wait_ge(gate_done, g + 1)
                nc.gpsimd.tensor_tensor(gate[:, 1:2], gate[:, 0:1], gate[:, 0:1], ALU.add).then_inc(gate_done, 1)
                for r in range(FH):
                    nc.gpsimd.indirect_dma_start(
                        out=raw[:, r // HALVES, ROW * (r % HALVES):ROW * (r % HALVES + 1)], out_offset=None,
                        in_=(lin_first, lin_last)[r % HALVES],
                        in_offset=bass.IndirectOffsetOnAxis(ap=idx[:, r:r + 1], axis=0)).then_inc(gathered, 16)

            gather(0)
            nc.gpsimd.memset(ident[:], 0.0).then_inc(w_zero, 1)
            pool.wait_ge(w_zero, 2)
            nc.gpsimd.affine_select(out=ident[:], in_=ident[:], compare_op=ALU.not_equal, fill=1.0, base=0,
                                    pattern=[[-1, P]], channel_multiplier=1).then_inc(id_ready, 1)
            with pool.Fori(1, G) as g:
                gather(g)

        @block.tensor
        def _(pe):
            def turn_embeddings(n, i):
                if i == 0:
                    pe.wait_ge(gathered, n * (16 * FH) + 16 * FH)
                wait(pe, et_copied, n * NET + i)
                for j in range(FPC):
                    f = FPC * i + j
                    mm = nc.tensor.transpose(ps[:, T_ET, P * j:P * (j + 1)],
                                             raw[:, f, 1:1 + HALVES * K], ident[:])
                mm.then_inc(et_done, 1)

            def hidden(g, k):
                for q in range(STEP * k, min(STEP * k + STEP, NQ)):
                    if q % CPT == 0:
                        pe.wait_ge(prod_ready, g * NT + (q // CPT + 1))
                    if q >= 2:
                        pe.wait_ge(hid_ready, g * NQ + (q - 1))
                    tile = prod[:, (q // CPT) % TRING, :]
                    nc.tensor.matmul(ps[:, Z[q % 2], :], w1_diag[:], tile[:, BANK * (q % CPT):BANK * (q % CPT + 1)],
                                     start=True, stop=True).then_inc(z_done, 1)

            def scores_and_dots(g, k):
                qs = range(STEP * k, min(STEP * k + STEP, NQ))
                n, t = k // SLOTS, k % SLOTS
                last = k == NS - 1 or t == SLOTS - 1
                if t == 0:
                    wait(pe, block_staged, g * (2 * NB) + 2 * (n - 1))
                for c, q in enumerate(qs):
                    tile = prod[:, (q // CPT) % TRING, :]
                    mm = nc.tensor.matmul(ps[32 * c:32 * c + 32, D[n % 2], :], wf_slot[:, 32 * t:32 * t + 32],
                                          tile[:, BANK * (q % CPT):BANK * (q % CPT + 1)],
                                          start=(t == 0), stop=last or (t == slots_of(n, c) - 1))
                    if q % CPT == CPT - 1:
                        mm.then_inc(prod_used, 1)
                pe.wait_ge(hid_ready, g * NQ + (qs[-1] + 1))
                for c, q in enumerate(qs):
                    mm = nc.tensor.matmul(ps[32 * c:32 * c + 32, S[n % 2], :], w2_slot[:, 32 * t:32 * t + 32],
                                          hid[:, q % HRING, :], start=(t == 0), stop=last or (t == slots_of(n, c) - 1))
                if last:
                    mm.then_inc(block_done, 1)

            def slots_of(n, c):
                return len([k for k in range(SLOTS * n, min(SLOTS * n + SLOTS, NS)) if STEP * k + c < NQ])

            def turn_block(g, n, which):
                pe.wait_ge(block_staged, g * (2 * NB) + (2 * n + which + 1))
                wait(pe, sg_copied, g * (4 * NB) + (4 * n + 2 * which))
                for j in range(FPC):
                    mm = nc.tensor.transpose(ps[:, T_SG, P * j:P * (j + 1)], stage[:, which, P * j:P * (j + 1)], ident[:])
                mm.then_inc(sg_done, 1)

            def body(g, first, last):
                for k in range(NS):
                    hidden(g, k)
                    if k > 0:
                        scores_and_dots(g, k - 1)
                    if not first and k in (2, 3):
                        turn_block(g - 1, NB - 1, k - 2)
                    if k in TURN_AT:
                        turn_block(g, *TURN_AT[k])
                    if not last and k in ET_AT:
                        turn_embeddings(g + 1, ET_AT[k])
                scores_and_dots(g, NS - 1)

            pe.wait_ge(id_ready, 1)
            for i in range(NET):
                turn_embeddings(0, i)
            pe.wait_ge(w_loaded, 16 * (4 * HALVES + 2))
            pe.wait_ge(w_ready, 2 * HALVES)
            over_groups(pe, body)
            for which in range(2):
                turn_block(G - 1, NB - 1, which)
            pe.wait_ge(prob_ready, 1)
            nc.tensor.transpose(ps[0:G * HALVES, T_SG, 0:P], prob[:], ident[:]).then_inc(y_turned, 1)

        @block.scalar
        def _(act):
            def copy_embeddings(n, i):
                act.wait_ge(et_done, n * NET + (i + 1))
                src = ps[:, T_ET, :]
                home = et[:, bass.ds(parity(n), 1), :].rearrange("p a x -> p (a x)")
                c = nc.scalar.copy(home[:, BANK * i:BANK * (i + 1)], src)
                if i < NDUP:
                    c = nc.scalar.copy(home[:, BANK * (i + NET):BANK * (i + NET + 1)], src)
                c.then_inc(et_copied, 1)

            def exponentials(g):
                act.wait_ge(tail, g * NTAIL + 6)
                nc.scalar.activation(pr1[:, 0], pr1[:, 0], ACT.Exp).then_inc(exp_done, 1)
                act.wait_ge(tail, g * NTAIL + 7)
                nc.scalar.activation(skewable(pr2[:, 0])[:, :, :, 0:F], skewable(pr2[:, 0])[:, :, :, 0:F],
                                     ACT.Exp).then_inc(exp_done, 1)

            def load_indices(n):
                act.wait_ge(lin_done, n * 1)
                nc.scalar.dma_start(idx[:], x_idx[bass.ds(n, 1)].rearrange("a p f -> (a p) f")).then_inc(idx_loaded, 16)

            def body(g, first, last):
                for k in range(NS):
                    if not last and k == LOAD_AT:
                        load_indices(g + 1)
                    for q in range(STEP * k, min(STEP * k + STEP, NQ)):
                        act.wait_ge(z_done, g * NQ + (q + 1))
                        nc.scalar.activation(hid[:, q % HRING, :], ps[:, Z[q % 2], :], ACT.Relu,
                                             bias=b1_col[:, 0:1]).then_inc(hid_ready, 1)
                    if not first and k == EXP_AT:
                        exponentials(g - 1)
                    if not last and k in ET_AT:
                        copy_embeddings(g + 1, ET_AT[k])

            for i in range(NET):
                copy_embeddings(0, i)
            act.wait_ge(w_loaded, 16 * (4 * HALVES + 2))
            over_groups(act, body)
            exponentials(G - 1)
            act.wait_ge(logit_ready, 1)
            nc.scalar.activation(prob[:], logit[:, 1, :], ACT.Sigmoid, bias=bf_col[:, 0:1]).then_inc(prob_ready, 1)

        @block.vector
        def _(dve):
            def product(g, j):
                d, i0 = (j * FPT) // F, (j * FPT) % F
                if j == 0:
                    dve.wait_ge(et_copied, g * NET + NET)
                wait(dve, prod_used, g * NT + (j - TRING + 1))
                home = et[:, bass.ds(parity(g), 1), :].rearrange("p a x -> p (a x)")
                nc.vector.tensor_tensor(prod[:, j % TRING, :], home[:, P * i0:P * (i0 + FPT)],
                                        home[:, P * (i0 + d):P * (i0 + d + FPT)], ALU.mult).then_inc(prod_ready, 1)

            def linear_part(n):
                dve.wait_ge(gathered, n * (16 * FH) + 16 * FH)
                nc.vector.tensor_reduce(linear[:, bass.ds(n * HALVES, HALVES)],
                                        raw[:, :, 0:HALVES * ROW:HALVES * ROW - 1].rearrange("p f h -> p h f"), AX_X,
                                        ALU.add).then_inc(lin_done, 1)

            def stage_block(g, n):
                dve.wait_ge(block_done, g * NB + (n + 1))
                wait(dve, sg_done, g * (2 * NB) + 2 * n)
                nc.vector.tensor_copy(stage[:, 0, :], ps[:, S[n % 2], :]).then_inc(block_staged, 1)
                nc.vector.tensor_copy(stage[:, 1, :], ps[:, D[n % 2], :]).then_inc(block_staged, 1)

            def unpack_block(g, n, which):
                slots = min(SLOTS, NS - SLOTS * n)
                dve.wait_ge(sg_done, g * (2 * NB) + (2 * n + which + 1))
                if n == 0 and which == 0:
                    wait(dve, tail, g * NTAIL)
                src = ps[:, T_SG, :].rearrange("p (i c h t) -> p i c h t", i=FPC, c=STEP, h=HALVES)
                for h in range(HALVES):
                    a = SLOTS * STEP * FPC * n
                    to = (score, dot)[which][:, h, a:a + slots * STEP * FPC]
                    to = to.rearrange("p (t c i) -> p i c t", c=STEP, i=FPC)
                    if which == 0:
                        nc.vector.tensor_scalar(to, src[:, :, :, h, 0:slots], b2_col[:, 0:1], None,
                                                ALU.add).then_inc(sg_copied, 1)
                    else:
                        nc.vector.tensor_copy(to, src[:, :, :, h, 0:slots]).then_inc(sg_copied, 1)

            def diagonals(t, a, b):
                return t[:, :, F * a:F * b].rearrange("p h (d i) -> p h d i", i=F)

            def softmax_step(g, s):
                def after(step):
                    dve.wait_ge(tail, g * NTAIL + (step + 1))

                if s == 0:
                    dve.wait_ge(sg_copied, g * (NB * 4) + NB * 4)
                    nc.vector.tensor_copy(skewable(sc2)[:, :, :, 0:F], diagonals(score, 1, NSK + 1)).then_inc(tail, 1)
                elif s == 1:
                    nc.vector.tensor_copy(skewable(sc2)[:, :, :, F:2 * F], diagonals(score, 1, NSK + 1)).then_inc(tail, 1)
                elif s == 2:
                    nc.vector.tensor_reduce(mx[:, 0], diagonals(score, 0, ND).rearrange("p h d i -> p h i d"), AX_X,
                                            ALU.max).then_inc(tail, 1)
                elif s == 3:
                    after(1)
                    nc.vector.tensor_reduce(mx[:, 1], skewed(sc2), AX_X, ALU.max).then_inc(tail, 1)
                elif s == 4:
                    after(3)
                    nc.vector.tensor_tensor(mrow[:, :, 0:F], mx[:, 0], mx[:, 1], ALU.max).then_inc(tail, 1)
                elif s == 5:
                    after(4)
                    nc.vector.tensor_tensor(
                        pr1[:, 0].rearrange("p h (d i) -> p h d i", i=F), diagonals(score, 0, ND),
                        mrow[:, :, 0:F].unsqueeze(2).to_broadcast([P, HALVES, ND, F]), ALU.subtract).then_inc(tail, 1)
                elif s == 6:
                    nc.vector.tensor_copy(mrow[:, :, F:FX], mrow[:, :, 0:FX - F]).then_inc(mrow_ext, 1)
                    dve.wait_ge(mrow_ext, g + 1)
                    row_of = bass.AP(tensor=mrow[:].tensor, offset=1, ap=[[HALVES * FX, P], [FX, HALVES], [1, NSK], [1, F]])
                    nc.vector.tensor_tensor(skewable(pr2[:, 0])[:, :, :, 0:F], diagonals(score, 1, NSK + 1), row_of,
                                            ALU.subtract).then_inc(tail, 1)
                elif s == 7:
                    dve.wait_ge(exp_done, g * 2 + 1)
                    nc.vector.tensor_tensor(pr1[:, 1], pr1[:, 0], dot[:, :, 0:ND * F], ALU.mult).then_inc(tail, 1)
                elif s == 8:
                    dve.wait_ge(exp_done, g * 2 + 2)
                    nc.vector.tensor_tensor(skewable(pr2[:, 1])[:, :, :, 0:F], skewable(pr2[:, 0])[:, :, :, 0:F],
                                            diagonals(dot, 1, NSK + 1), ALU.mult).then_inc(tail, 1)
                elif s == 9:
                    after(8)
                    v = skewable(pr2[:].rearrange("p w h x -> p (w h) x"))
                    nc.vector.tensor_copy(v[:, :, :, F:2 * F], v[:, :, :, 0:F]).then_inc(tail, 1)
                elif s == 10:
                    nc.vector.tensor_reduce(zn[:, 0], pr1[:].rearrange("p w h (d i) -> p (w h) i d", i=F), AX_X,
                                            ALU.add).then_inc(tail, 1)
                elif s == 11:
                    after(9)
                    nc.vector.tensor_reduce(zn[:, 1], skewed(pr2[:].rearrange("p w h x -> p (w h) x")), AX_X,
                                            ALU.add).then_inc(tail, 1)
                elif s == 12:
                    after(11)
                    nc.vector.tensor_tensor(zn[:, 2], zn[:, 0], zn[:, 1], ALU.add).then_inc(tail, 1)
                elif s == 13:
                    after(12)
                    nc.vector.reciprocal(rz[:], zn[:, 2, 0:HALVES]).then_inc(tail, 1)
                elif s == 14:
                    after(13)
                    nc.vector.tensor_tensor(share[:], zn[:, 2, HALVES:2 * HALVES], rz[:], ALU.mult).then_inc(share_done, 1)
                    dve.wait_ge(share_done, g + 1)
                    nc.vector.tensor_reduce(inter[:, bass.ds(g * HALVES, HALVES)], share[:], AX_X,
                                            ALU.add).then_inc(tail, 1)

            SOFTMAX_AT = {5: (0, 1), 6: (2,), 7: (3,), 8: (4, 5), 9: (6,), 11: (7,), 12: (8,), 13: (9,), 14: (10,),
                          15: (11, 12, 13, 14)}

            def body(g, first, last):
                j = 0
                for k in range(NS):
                    while j < NT and j <= STEP * k // CPT + TRING - 1:
                        product(g, j)
                        j += 1
                    if not first:
                        if k == 0:
                            stage_block(g - 1, NB - 1)
                        if k in (2, 3):
                            unpack_block(g - 1, NB - 1, k - 2)
                        for s in SOFTMAX_AT.get(k, ()):
                            softmax_step(g - 1, s)
                    if k in STAGE_AT:
                        stage_block(g, STAGE_AT[k])
                    if k in TURN_AT:
                        unpack_block(g, *TURN_AT[k])
                    if not last and k == LIN_AT:
                        linear_part(g + 1)

            nc.vector.memset(w2_slot[:], 0.0).then_inc(slot_zero, 1)
            nc.vector.memset(wf_slot[:], 0.0).then_inc(slot_zero, 1)
            dve.wait_ge(slot_zero, 2)
            dve.wait_ge(w_loaded, 16 * (4 * HALVES + 2))
            for slot, col in ((w2_slot, w2_col), (wf_slot, wf_col)):
                for h in range(HALVES):
                    half = slice(K * h, K * (h + 1))
                    to = bass.AP(tensor=slot[:].tensor, offset=K * h * SLOTS * 32 + SLOTS * h,
                                 ap=[[SLOTS * 32, K], [33, SLOTS]])
                    nc.vector.tensor_copy(to, col[half, 0:1].to_broadcast([K, SLOTS])).then_inc(w_ready, 1)
            linear_part(0)
            over_groups(dve, body)
            stage_block(G - 1, NB - 1)
            for which in range(2):
                unpack_block(G - 1, NB - 1, which)
            for s in range(NTAIL):
                softmax_step(G - 1, s)
            dve.wait_ge(tail, G * NTAIL)
            dve.wait_ge(lin_done, G)
            nc.vector.tensor_tensor(logit[:, 1, :], inter[:], linear[:], ALU.add).then_inc(logit_ready, 1)
            dve.wait_ge(y_turned, 1)
            nc.vector.tensor_copy(y_rows[:], ps[0:G * HALVES, T_SG, 0:P]).then_inc(y_ready, 1)


def kernel(**inputs):
    import numpy as np
    import concourse.bacc as bacc
    from concourse.bass_utils import run_bass_kernel_spmd

    x = np.asarray(inputs["r_x"])
    batch, fields = x.shape
    groups = batch // (HALVES * P)
    x = x.reshape(groups, HALVES, P, fields).transpose(0, 2, 3, 1).reshape(groups, P, fields * HALVES)
    V, lin = inputs["L0_rec_V_table"], inputs["L0_rec_lin_table"]
    arrays = {"x_idx": x, "lin_first": np.concatenate([lin, V], axis=1), "lin_last": np.concatenate([V, lin], axis=1)}
    for name in ("W1", "b1", "W2", "b2", "Wf", "bf"):
        arrays[name] = inputs["L0_rec_" + name]
    arrays = {n: np.ascontiguousarray(a) for n, a in arrays.items()}

    nc = bacc.Bacc("TRN2", target_bir_lowering=False, num_devices=1)
    args = [nc.dram_tensor(n, a.shape, mybir.dt.from_np(a.dtype), kind="ExternalInput").ap() for n, a in arrays.items()]
    args.append(nc.dram_tensor("y", (batch,), F32, kind="ExternalOutput").ap())
    attentional_fm(nc, *args)
    r = run_bass_kernel_spmd(nc, [arrays], core_ids=[0])
    return r.results[0]["y"]
```

```python
from contextlib import ExitStack

import concourse.bass as bass
from concourse import mybir

ALU = mybir.AluOpType
ACT = mybir.ActivationFunctionType
F32 = mybir.dt.float32
F32R = mybir.dt.float32r
I32 = mybir.dt.int32
AX_X = mybir.AxisListType.X

P = 128
BANK = 512
HALVES = 2


def attentional_fm(nc, x_idx, lin_first, lin_last, W1, b1, W2, b2, Wf, bf, out):
    G, _, FH = x_idx.shape
    F = FH // HALVES
    K = W1.shape[0]
    ROW = K + 1
    ND = F // 2 + 1
    NSK = F // 2 - 1
    FPC = BANK // P
    NQ = ND * F // FPC
    CPT = 5
    NT = NQ // CPT
    FPT = CPT * FPC
    TRING = 3
    HRING = 10
    STEP = 4
    NS = -(-NQ // STEP)
    SLOTS = 32 // HALVES
    NB = -(-NS // SLOTS)
    QPAD = NS * STEP
    NET = F // FPC
    FX = F + F // 2
    NTAIL = 18
    SKEW = NSK * 2 * F
    LRING = 2
    SOFTMAX_AT = {9: (0, 1, 2), 13: (3, 4, 5), 16: (6, 7, 8), 19: (9, 10, 11), 22: (12,), 23: (13, 14, 15, 16, 17)}
    whole = {0, 5, 9, 13, 16, 19, 22, NT - 1}
    assert 2 * K == P and NQ % CPT == 0 and NT % TRING == 0 and NT % LRING == 0 and NQ % HRING == 0
    assert F % FPT == 0 and FPT * 2 == F and NQ % 3 == 0
    assert lin_first.shape[1] == lin_last.shape[1] == ROW

    with ExitStack() as ctx:
        def sb(name, shape, dt=F32):
            return ctx.enter_context(nc.sbuf_tensor(name, shape, dt))

        def sem(name):
            return ctx.enter_context(nc.semaphore(name))

        w1_diag = sb("w1_diag", [P, P])
        w1_hi = sb("w1_hi", [P, P], F32R)
        w1_lo = sb("w1_lo", [P, P], F32R)
        w2_slot = sb("w2_slot", [P, SLOTS * 32])
        wf_slot = sb("wf_slot", [P, SLOTS * 32])
        w2_col = sb("w2_col", [P, 1])
        wf_col = sb("wf_col", [P, 1])
        b1_col = sb("b1_col", [P, 1])
        b2_col = sb("b2_col", [P, 1])
        bf_col = sb("bf_col", [P, 1])
        ident = sb("ident", [P, P])
        idx = sb("idx", [P, FH], I32)
        gate = sb("gate", [P, 2])
        raw = sb("raw", [P, F, HALVES * ROW])
        et = sb("et", [P, 2, F * P])
        prod = sb("prod", [P, TRING, FPT * P])
        prod_hi = sb("prod_hi", [P, TRING, FPT * P], F32R)
        prod_lo = sb("prod_lo", [P, LRING, FPT * P], F32R)
        hid = sb("hid", [P, HRING, BANK])
        stage = sb("stage", [P, 2, BANK])
        pair = sb("pair", [P, 2, HALVES, QPAD * FPC])
        back = sb("back", [P, HALVES, SKEW + F])
        mx = sb("mx", [P, 2, HALVES, F])
        mrow = sb("mrow", [P, HALVES, FX])
        zn = sb("zn", [P, 3, 2 * HALVES, F])
        rz = sb("rz", [P, HALVES, F])
        share = sb("share", [P, HALVES, F])
        inter = sb("inter", [P, G * HALVES])
        linear = sb("linear", [P, G * HALVES])
        logit = sb("logit", [P, 2, G * HALVES])
        prob = sb("prob", [P, G * HALVES])
        y_rows = sb("y_rows", [G * HALVES, P])
        ps = ctx.enter_context(nc.psum_tensor("ps", [P, 8, BANK], F32))
        Z, S, D, T = (0, 1, 2), (3, 4), (5, 6), 7

        w_zero = sem("w_zero")
        w_loaded = sem("w_loaded")
        w_ready = sem("w_ready")
        w1_rounded = sem("w1_rounded")
        id_ready = sem("id_ready")
        gate_done = sem("gate_done")
        idx_loaded = sem("idx_loaded")
        first_rows = [sem(f"first_rows{i}") for i in range(NET)]
        gathered = sem("gathered")
        lin_done = sem("lin_done")
        et_done = sem("et_done")
        et_copied = sem("et_copied")
        prod_ready = sem("prod_ready")
        hi_ready = sem("hi_ready")
        lo_ready = sem("lo_ready")
        prod_used = sem("prod_used")
        z_done = sem("z_done")
        hid_ready = sem("hid_ready")
        block_done = sem("block_done")
        block_staged = sem("block_staged")
        sg_done = sem("sg_done")
        sg_copied = sem("sg_copied")
        tail = sem("tail")
        row_max = sem("row_max")
        slot_zero = sem("slot_zero")
        exp_done = sem("exp_done")
        logit_ready = sem("logit_ready")
        prob_ready = sem("prob_ready")
        y_turned = sem("y_turned")
        y_ready = sem("y_ready")
        stored = sem("stored")

        block = ctx.enter_context(nc.Block())

        def wait(eng, s, value):
            if not isinstance(value, int) or value > 0:
                eng.wait_ge(s, value)

        def over_groups(eng, body):
            body(0, True, False)
            with eng.Fori(1, G - 1) as g:
                body(g, False, False)
            body(G - 1, False, True)

        def parity(g):
            return g % 2 if isinstance(g, int) else g & 1

        def skewable(t):
            return t[:, :, 0:SKEW].rearrange("p h (d x) -> p h d x", x=2 * F)

        def skewed(t):
            return t[:, :, F - 1:F - 1 + NSK * (2 * F - 1)].rearrange("p h (d x) -> p h x d", x=2 * F - 1)[:, :, 0:F, :]

        STAGE_AT = {18: 0, 33: 1, 48: 2}
        STAGE_LAST_AT = 2
        TURN_AT = {31: (0, 0), 32: (0, 1), 42: (1, 0), 43: (1, 1), 51: (2, 0), 52: (2, 1)}
        TURN_LAST_AT = {4: 0, 7: 1}
        ET_AT = {k: i for i, k in enumerate((22, 23, 25, 26, 27, 28, 36, 37, 38, 41))}
        LIN_AT = 28
        LOAD_AT = 0
        EXP_AT = {17: 1, 21: 0}
        assert NB == 4 and len(ET_AT) == NET
        for at, n in STAGE_AT.items():
            assert SLOTS * (n + 1) <= at < SLOTS * (n + 2) - 1
            assert all(k < at for k, (m, _) in TURN_AT.items() if m < n) and all(k > at for k, (m, _) in TURN_AT.items() if m == n)

        def split_before(g, j):
            return g * (NT - len(whole)) + len([t for t in range(j) if t not in whole])

        def rows_there(eng, n):
            if isinstance(n, int) and n == 0:
                for s in first_rows:
                    eng.wait_ge(s, 16 * FPC * HALVES)
            else:
                eng.wait_ge(gathered, n * (16 * FH))

        @block.sync
        def _(sp):
            sp.wait_ge(w_zero, 1)
            for h in range(HALVES):
                half = slice(K * h, K * (h + 1))
                sp.dma_start(w1_diag[half, half], W1).then_inc(w_loaded, 16)
                sp.dma_start(w2_col[half, :], W2).then_inc(w_loaded, 16)
                sp.dma_start(wf_col[half, :], Wf).then_inc(w_loaded, 16)
                sp.dma_start(b1_col[half, :], b1.rearrange("(a o) -> a o", o=1)).then_inc(w_loaded, 16)
            sp.dma_start(b2_col[:], b2.rearrange("(a o) -> a o", o=1).to_broadcast([P, 1])).then_inc(w_loaded, 16)
            sp.dma_start(bf_col[:], bf.rearrange("(a o) -> a o", o=1).to_broadcast([P, 1])).then_inc(w_loaded, 16)
            sp.dma_start(idx[:], x_idx[0]).then_inc(idx_loaded, 16)
            sp.wait_ge(y_ready, 1)
            sp.dma_start(out.rearrange("(c p) -> c p", p=P), y_rows[:]).then_inc(stored, 16)
            sp.wait_ge(stored, 16)

        @block.gpsimd
        def _(pool):
            nc.gpsimd.memset(gate[:], 0.0).then_inc(gate_done, 1)
            pool.wait_ge(gate_done, 1)
            nc.gpsimd.memset(w1_diag[:], 0.0).then_inc(w_zero, 1)


            def gather(g, first=False):
                pool.wait_ge(idx_loaded, g * 16 + 16)
                pool.wait_ge(gate_done, g + 1)
                nc.gpsimd.tensor_tensor(gate[:, 1:2], gate[:, 0:1], gate[:, 0:1], ALU.add).then_inc(gate_done, 1)
                for r in range(FH):
                    nc.gpsimd.indirect_dma_start(
                        out=raw[:, r // HALVES, ROW * (r % HALVES):ROW * (r % HALVES + 1)], out_offset=None,
                        in_=(lin_first, lin_last)[r % HALVES],
                        in_offset=bass.IndirectOffsetOnAxis(ap=idx[:, r:r + 1], axis=0)).then_inc(
                            first_rows[r // (FPC * HALVES)] if first else gathered, 16)

            nc.gpsimd.memset(ident[:], 0.0).then_inc(w_zero, 1)
            pool.wait_ge(w_zero, 2)
            nc.gpsimd.affine_select(out=ident[:], in_=ident[:], compare_op=ALU.not_equal, fill=1.0, base=0,
                                    pattern=[[-1, P]], channel_multiplier=1).then_inc(id_ready, 1)
            gather(0, first=True)
            with pool.Fori(1, G) as g:
                gather(g)

        @block.tensor
        def _(pe):
            def turn_embeddings(n, i):
                if isinstance(n, int) and n == 0:
                    pe.wait_ge(first_rows[i], 16 * FPC * HALVES)
                else:
                    if i == 0:
                        pe.wait_ge(gathered, n * (16 * FH))
                    before = len([k for k in TURN_AT if k < min(k for k in ET_AT if ET_AT[k] == i)])
                    wait(pe, sg_copied, (n - 1) * (4 * NB) + 2 * before)
                wait(pe, et_copied, n * NET + i)
                for j in range(FPC):
                    f = FPC * i + j
                    mm = nc.tensor.transpose(ps[:, T, P * j:P * (j + 1)], raw[:, f, 1:1 + HALVES * K], ident[:])
                mm.then_inc(et_done, 1)

            def hidden(g, k):
                for q in range(STEP * k, min(STEP * k + STEP, NQ)):
                    j, at = q // CPT, slice(BANK * (q % CPT), BANK * (q % CPT + 1))
                    if q % CPT == 0 and j not in whole:
                        pe.wait_ge(lo_ready, split_before(g, j) + 1)
                    if q >= 3:
                        pe.wait_ge(hid_ready, g * NQ + (q - 2))
                    z = ps[:, Z[q % 3], :]
                    if j in whole:
                        mm = nc.tensor.matmul(z, w1_diag[:], prod[:, j % TRING, at], start=True, stop=True)
                    else:
                        hi, lo = prod_hi[:, j % TRING, at], prod_lo[:, j % LRING, at]
                        nc.tensor.matmul(z, w1_hi[:], hi, start=True, stop=False)
                        nc.tensor.matmul(z, w1_hi[:], lo, start=False, stop=False)
                        mm = nc.tensor.matmul(z, w1_lo[:], hi, start=False, stop=True)
                    mm.then_inc(z_done, 1)

            def dots(g, k):
                n, t = k // SLOTS, k % SLOTS
                if t == 0:
                    wait(pe, block_staged, g * (2 * NB) + 2 * (n - 1))
                for c, q in enumerate(range(STEP * k, min(STEP * k + STEP, NQ))):
                    if q % CPT == 0:
                        pe.wait_ge(prod_ready, g * NT + (q // CPT + 1))
                    mm = nc.tensor.matmul(ps[32 * c:32 * c + 32, D[n % 2], :], wf_slot[:, 32 * t:32 * t + 32],
                                          prod[:, (q // CPT) % TRING, BANK * (q % CPT):BANK * (q % CPT + 1)],
                                          start=(t == 0), stop=(t == slots_of(n, c) - 1))
                    if q % CPT == CPT - 1:
                        mm.then_inc(prod_used, 1)

            def scores(g, k):
                n, t = k // SLOTS, k % SLOTS
                qs = range(STEP * k, min(STEP * k + STEP, NQ))
                pe.wait_ge(hid_ready, g * NQ + (qs[-1] + 1))
                for c, q in enumerate(qs):
                    mm = nc.tensor.matmul(ps[32 * c:32 * c + 32, S[n % 2], :], w2_slot[:, 32 * t:32 * t + 32],
                                          hid[:, q % HRING, :], start=(t == 0), stop=(t == slots_of(n, c) - 1))
                if t == SLOTS - 1 or k == NS - 1:
                    mm.then_inc(block_done, 1)

            def slots_of(n, c):
                return len([k for k in range(SLOTS * n, min(SLOTS * n + SLOTS, NS)) if STEP * k + c < NQ])

            def turn_block(g, n, which, after_et):
                pe.wait_ge(block_staged, g * (2 * NB) + (2 * n + which + 1))
                wait(pe, sg_copied, g * (4 * NB) + (4 * n + 2 * which))
                pe.wait_ge(et_copied, after_et)
                for j in range(FPC):
                    mm = nc.tensor.transpose(ps[:, T, P * j:P * (j + 1)], stage[:, which, P * j:P * (j + 1)], ident[:])
                mm.then_inc(sg_done, 1)

            def body(g, first, last):
                dots(g, 0)
                for k in range(NS):
                    hidden(g, k)
                    if k + 1 < NS - 1:
                        dots(g, k + 1)
                    if k > 0:
                        scores(g, k - 1)
                    if not first and k in TURN_LAST_AT:
                        turn_block(g - 1, NB - 1, TURN_LAST_AT[k], g * NET + NET)
                    if k in TURN_AT:
                        n, which = TURN_AT[k]
                        later = 0 if last else len([e for e in ET_AT if e < k])
                        turn_block(g, n, which, g * NET + (NET + later))
                    if not last and k in ET_AT:
                        turn_embeddings(g + 1, ET_AT[k])
                dots(g, NS - 1)
                scores(g, NS - 1)

            pe.wait_ge(id_ready, 1)
            for i in range(NET):
                turn_embeddings(0, i)
            pe.wait_ge(w_loaded, 16 * (4 * HALVES + 2))
            pe.wait_ge(w_ready, 2 * HALVES + 1)
            over_groups(pe, body)
            for which in range(2):
                turn_block(G - 1, NB - 1, which, G * NET)
            pe.wait_ge(prob_ready, 1)
            nc.tensor.transpose(ps[0:G * HALVES, T, 0:P], prob[:], ident[:]).then_inc(y_turned, 1)

        @block.scalar
        def _(act):
            def copy_embeddings(n, i):
                act.wait_ge(et_done, n * NET + (i + 1))
                home = et[:, bass.ds(parity(n), 1), :].rearrange("p a x -> p (a x)")
                nc.scalar.copy(home[:, BANK * i:BANK * (i + 1)], ps[:, T, :]).then_inc(et_copied, 1)

            def round_tile(g, j):
                act.wait_ge(prod_ready, g * NT + (j + 1))
                wait(act, z_done, g * NQ + CPT * (j - TRING + 1))
                nc.scalar.copy(prod_hi[:, j % TRING, :], prod[:, j % TRING, :]).then_inc(hi_ready, 1)

            def stage_block(g, n):
                act.wait_ge(block_done, g * NB + (n + 1))
                wait(act, sg_done, g * (2 * NB) + 2 * n)
                nc.scalar.copy(stage[:, 0, :], ps[:, S[n % 2], :]).then_inc(block_staged, 1)
                nc.scalar.copy(stage[:, 1, :], ps[:, D[n % 2], :]).then_inc(block_staged, 1)

            def unpack_block(g, n, which):
                slots = min(SLOTS, NS - SLOTS * n)
                act.wait_ge(sg_done, g * (2 * NB) + (2 * n + which + 1))
                if n == 0 and which == 0:
                    wait(act, tail, g * NTAIL)
                src = ps[:, T, :].rearrange("p (i c h t) -> p i c h t", i=FPC, c=STEP, h=HALVES)
                for h in range(HALVES):
                    a = SLOTS * STEP * FPC * n
                    to = pair[:, which, h, a:a + slots * STEP * FPC].rearrange("p (t c i) -> p i c t", c=STEP, i=FPC)
                    if which == 0:
                        nc.scalar.activation(to, src[:, :, :, h, 0:slots], ACT.Identity,
                                             bias=b2_col[:, 0:1]).then_inc(sg_copied, 1)
                    else:
                        nc.scalar.copy(to, src[:, :, :, h, 0:slots]).then_inc(sg_copied, 1)

            def exponentials(g, which):
                if which == 1:
                    act.wait_ge(tail, g * NTAIL + 6)
                    v = skewable(back)[:, :, :, 0:F]
                else:
                    act.wait_ge(tail, g * NTAIL + 7)
                    v = pair[:, 0, :, 0:ND * F]
                nc.scalar.activation(v, v, ACT.Exp).then_inc(exp_done, 1)

            def load_indices(n):
                act.wait_ge(lin_done, n * 1)
                nc.scalar.dma_start(idx[:], x_idx[bass.ds(n, 1)].rearrange("a p f -> (a p) f")).then_inc(idx_loaded, 16)

            def body(g, first, last):
                for k in range(NS):
                    if not last and k == LOAD_AT:
                        load_indices(g + 1)
                    if k == 0:
                        round_tile(g, 1)
                    for q in range(STEP * k, min(STEP * k + STEP, NQ)):
                        act.wait_ge(z_done, g * NQ + (q + 1))
                        nc.scalar.activation(hid[:, q % HRING, :], ps[:, Z[q % 3], :], ACT.Relu,
                                             bias=b1_col[:, 0:1]).then_inc(hid_ready, 1)
                    for j in range(2, NT):
                        if j not in whole and (CPT * (j - 2) + 2) // STEP == k:
                            round_tile(g, j)
                    if k in STAGE_AT:
                        stage_block(g, STAGE_AT[k])
                    if k in TURN_AT:
                        unpack_block(g, *TURN_AT[k])
                    if not first:
                        if k == STAGE_LAST_AT:
                            stage_block(g - 1, NB - 1)
                        if k in TURN_LAST_AT:
                            unpack_block(g - 1, NB - 1, TURN_LAST_AT[k])
                        if k in EXP_AT:
                            exponentials(g - 1, EXP_AT[k])
                    if not last and k in ET_AT:
                        copy_embeddings(g + 1, ET_AT[k])

            act.wait_ge(w_loaded, 16 * (4 * HALVES + 2))
            nc.scalar.copy(w1_hi[:], w1_diag[:]).then_inc(w1_rounded, 1)
            for i in range(NET):
                copy_embeddings(0, i)
            over_groups(act, body)
            stage_block(G - 1, NB - 1)
            for which in range(2):
                unpack_block(G - 1, NB - 1, which)
            exponentials(G - 1, 1)
            exponentials(G - 1, 0)
            act.wait_ge(logit_ready, 1)
            nc.scalar.activation(prob[:], logit[:, 1, :], ACT.Sigmoid, bias=bf_col[:, 0:1]).then_inc(prob_ready, 1)

        @block.vector
        def _(dve):
            def product(g, j):
                d, i0 = (j * FPT) // F, (j * FPT) % F
                if j == 0:
                    dve.wait_ge(et_copied, g * NET + NET)
                wait(dve, prod_used, g * NT + (j - TRING + 1))
                if (j - TRING) % NT in whole:
                    wait(dve, z_done, g * NQ + CPT * (j - TRING + 1))
                home = et[:, bass.ds(parity(g), 1), :].rearrange("p a x -> p (a x)")
                straight = min(FPT, F - i0 - d)
                for a, b, to in ((0, straight, i0 + d), (straight, FPT, 0)):
                    if a < b:
                        ins = nc.vector.tensor_tensor(prod[:, j % TRING, P * a:P * b], home[:, P * (i0 + a):P * (i0 + b)],
                                                      home[:, P * to:P * (to + b - a)], ALU.mult)
                ins.then_inc(prod_ready, 1)

            def rest_of_tile(g, j):
                dve.wait_ge(hi_ready, split_before(g, j) + 1)
                wait(dve, z_done, g * NQ + CPT * (j - LRING + 1))
                dve.wait_ge(prod_ready, g * NT + (j + 1))
                nc.vector.tensor_tensor(prod_lo[:, j % LRING, :], prod[:, j % TRING, :],
                                        prod_hi[:, j % TRING, :].bitcast(F32), ALU.subtract).then_inc(lo_ready, 1)

            def linear_part(n):
                rows_there(dve, n)
                nc.vector.tensor_reduce(linear[:, bass.ds(n * HALVES, HALVES)],
                                        raw[:, :, 0:HALVES * ROW:HALVES * ROW - 1].rearrange("p f h -> p h f"), AX_X,
                                        ALU.add).then_inc(lin_done, 1)

            def diagonals(which, a, b):
                return pair[:, which, :, F * a:F * b].rearrange("p h (d i) -> p h d i", i=F)

            def softmax_step(g, s):
                def after(step):
                    dve.wait_ge(tail, g * NTAIL + (step + 1))

                once, again = skewable(back)[:, :, :, 0:F], skewable(back)[:, :, :, F:2 * F]
                if s == 0:
                    dve.wait_ge(sg_copied, g * (NB * 4) + NB * 4)
                    ins = nc.vector.tensor_copy(once, diagonals(0, 1, NSK + 1))
                elif s == 1:
                    ins = nc.vector.tensor_copy(again, diagonals(0, 1, NSK + 1))
                elif s == 2:
                    ins = nc.vector.tensor_reduce(mx[:, 0], diagonals(0, 0, ND).rearrange("p h d i -> p h i d"), AX_X,
                                                  ALU.max)
                elif s == 3:
                    after(1)
                    ins = nc.vector.tensor_reduce(mx[:, 1], skewed(back), AX_X, ALU.max)
                elif s == 4:
                    after(3)
                    nc.vector.tensor_tensor(mrow[:, :, 0:F], mx[:, 0], mx[:, 1], ALU.max).then_inc(row_max, 1)
                    dve.wait_ge(row_max, g + 1)
                    ins = nc.vector.tensor_copy(mrow[:, :, F:FX], mrow[:, :, 0:FX - F])
                elif s == 5:
                    after(4)
                    row_of = bass.AP(tensor=mrow[:].tensor, offset=1, ap=[[HALVES * FX, P], [FX, HALVES], [1, NSK], [1, F]])
                    ins = nc.vector.tensor_tensor(once, diagonals(0, 1, NSK + 1), row_of, ALU.subtract)
                elif s == 6:
                    after(5)
                    ins = nc.vector.tensor_tensor(diagonals(0, 0, ND), diagonals(0, 0, ND),
                                                  mrow[:, :, 0:F].unsqueeze(2).to_broadcast([P, HALVES, ND, F]),
                                                  ALU.subtract)
                elif s == 7:
                    dve.wait_ge(exp_done, g * 2 + 1)
                    ins = nc.vector.tensor_copy(again, once)
                elif s == 8:
                    after(7)
                    ins = nc.vector.tensor_reduce(zn[:, 1, 0:HALVES], skewed(back), AX_X, ALU.add)
                elif s == 9:
                    after(8)
                    ins = nc.vector.tensor_tensor(once, once, diagonals(1, 1, NSK + 1), ALU.mult)
                elif s == 10:
                    after(9)
                    ins = nc.vector.tensor_copy(again, once)
                elif s == 11:
                    after(10)
                    ins = nc.vector.tensor_reduce(zn[:, 1, HALVES:2 * HALVES], skewed(back), AX_X, ALU.add)
                elif s == 12:
                    dve.wait_ge(exp_done, g * 2 + 2)
                    ins = nc.vector.tensor_tensor(pair[:, 1, :, 0:ND * F], pair[:, 0, :, 0:ND * F],
                                                  pair[:, 1, :, 0:ND * F], ALU.mult)
                elif s == 13:
                    after(12)
                    v = pair[:, :, :, 0:ND * F].rearrange("p w h x -> p (w h) x").rearrange("p w (d i) -> p w i d", i=F)
                    ins = nc.vector.tensor_reduce(zn[:, 0], v, AX_X, ALU.add)
                elif s == 14:
                    after(13)
                    ins = nc.vector.tensor_tensor(zn[:, 2], zn[:, 0], zn[:, 1], ALU.add)
                elif s == 15:
                    after(14)
                    ins = nc.vector.reciprocal(rz[:], zn[:, 2, 0:HALVES])
                elif s == 16:
                    after(15)
                    ins = nc.vector.tensor_tensor(share[:], zn[:, 2, HALVES:2 * HALVES], rz[:], ALU.mult)
                elif s == 17:
                    after(16)
                    ins = nc.vector.tensor_reduce(inter[:, bass.ds(g * HALVES, HALVES)], share[:], AX_X, ALU.add)
                ins.then_inc(tail, 1)

            def body(g, first, last):
                for j in range(NT):
                    product(g, j)
                    if j > 0 and j - 1 not in whole:
                        rest_of_tile(g, j - 1)
                    if not first:
                        for s in SOFTMAX_AT.get(j, ()):
                            softmax_step(g - 1, s)
                    if not last and j == LIN_AT:
                        linear_part(g + 1)

            dve.wait_ge(w1_rounded, 1)
            nc.vector.tensor_tensor(w1_lo[:], w1_diag[:], w1_hi[:].bitcast(F32), ALU.subtract).then_inc(w_ready, 1)
            nc.vector.memset(w2_slot[:], 0.0).then_inc(slot_zero, 1)
            nc.vector.memset(wf_slot[:], 0.0).then_inc(slot_zero, 1)
            dve.wait_ge(slot_zero, 2)
            dve.wait_ge(w_loaded, 16 * (4 * HALVES + 2))
            for slot, col in ((w2_slot, w2_col), (wf_slot, wf_col)):
                for h in range(HALVES):
                    half = slice(K * h, K * (h + 1))
                    to = bass.AP(tensor=slot[:].tensor, offset=K * h * SLOTS * 32 + SLOTS * h,
                                 ap=[[SLOTS * 32, K], [33, SLOTS]])
                    nc.vector.tensor_copy(to, col[half, 0:1].to_broadcast([K, SLOTS])).then_inc(w_ready, 1)
            linear_part(0)
            over_groups(dve, body)
            for s in range(NTAIL):
                softmax_step(G - 1, s)
            dve.wait_ge(tail, G * NTAIL)
            dve.wait_ge(lin_done, G)
            nc.vector.tensor_tensor(logit[:, 1, :], inter[:], linear[:], ALU.add).then_inc(logit_ready, 1)
            dve.wait_ge(y_turned, 1)
            nc.vector.tensor_copy(y_rows[:], ps[0:G * HALVES, T, 0:P]).then_inc(y_ready, 1)


def kernel(**inputs):
    import numpy as np
    import concourse.bacc as bacc
    from concourse.bass_utils import run_bass_kernel_spmd

    x = np.asarray(inputs["r_x"])
    batch, fields = x.shape
    groups = batch // (HALVES * P)
    x = x.reshape(groups, HALVES, P, fields).transpose(0, 2, 3, 1).reshape(groups, P, fields * HALVES)
    V, lin = inputs["L0_rec_V_table"], inputs["L0_rec_lin_table"]
    arrays = {"x_idx": x, "lin_first": np.concatenate([lin, V], axis=1), "lin_last": np.concatenate([V, lin], axis=1)}
    for name in ("W1", "b1", "W2", "b2", "Wf", "bf"):
        arrays[name] = inputs["L0_rec_" + name]
    arrays = {n: np.ascontiguousarray(a) for n, a in arrays.items()}

    nc = bacc.Bacc("TRN2", target_bir_lowering=False, num_devices=1)
    args = [nc.dram_tensor(n, a.shape, mybir.dt.from_np(a.dtype), kind="ExternalInput").ap() for n, a in arrays.items()]
    args.append(nc.dram_tensor("y", (batch,), F32, kind="ExternalOutput").ap())
    attentional_fm(nc, *args)
    r = run_bass_kernel_spmd(nc, [arrays], core_ids=[0])
    return r.results[0]["y"]
```

```python
from contextlib import ExitStack

import concourse.bass as bass
from concourse import mybir

ALU = mybir.AluOpType
ACT = mybir.ActivationFunctionType
F32 = mybir.dt.float32
F32R = mybir.dt.float32r
I32 = mybir.dt.int32
AX_X = mybir.AxisListType.X

P = 128
BANK = 512
HALVES = 2


def attentional_fm(nc, x_idx, lin_first, lin_last, W1, b1, W2, b2, Wf, bf, out):
    G, _, FH = x_idx.shape
    F = FH // HALVES
    K = W1.shape[0]
    ROW = K + 1
    ND = F // 2 + 1
    NSK = F // 2 - 1
    FPC = BANK // P
    NQ = ND * F // FPC
    CPT = 5
    NT = NQ // CPT
    FPT = CPT * FPC
    SIDES = F // FPT
    TRING = 3
    HRING = 10
    STEP = 4
    NS = -(-NQ // STEP)
    SLOTS = 32 // HALVES
    NB = -(-NS // SLOTS)
    QPAD = NS * STEP
    NET = F // FPC
    FX = F + F // 2
    NTAIL = 18
    SKEW = NSK * 2 * F
    LRING = 2
    SOFTMAX_AT = {8: (0,), 10: (1,), 11: (2,), 12: (3,), 13: (4,), 16: (5, 6,), 19: (7, 8, 9,), 20: (10,), 24: (11,), 28: (12, 13,), 32: (14, 15, 16, 17,)}
    whole = {10, 15, 18, 27}
    own = {1}
    ROUND_CUT = 3
    ROUND_AT = (2, 4)
    shifted = {8, 10, 16, 24, 29, 31}
    SHIFTED_AT = (1, 4)
    assert 2 * K == P and NQ % CPT == 0 and NT % TRING == 0 and NT % LRING == 0 and NQ % HRING == 0
    assert SIDES == 2 and SIDES * FPT == F and NT == SIDES * ND and NQ % 3 == 0
    assert lin_first.shape[1] == lin_last.shape[1] == ROW

    with ExitStack() as ctx:
        def sb(name, shape, dt=F32):
            return ctx.enter_context(nc.sbuf_tensor(name, shape, dt))

        def sem(name):
            return ctx.enter_context(nc.semaphore(name))

        w1_diag = sb("w1_diag", [P, P])
        w1_hi = sb("w1_hi", [P, P], F32R)
        w1_lo = sb("w1_lo", [P, P], F32R)
        w2_slot = sb("w2_slot", [P, SLOTS * 32])
        wf_slot = sb("wf_slot", [P, SLOTS * 32])
        w2_col = sb("w2_col", [P, 1])
        wf_col = sb("wf_col", [P, 1])
        b1_col = sb("b1_col", [P, 1])
        b2_col = sb("b2_col", [P, 1])
        bf_col = sb("bf_col", [P, 1])
        ident = sb("ident", [P, P])
        idx = sb("idx", [P, FH], I32)
        gate = sb("gate", [P, 2])
        raw = sb("raw", [P, F, HALVES * ROW])
        et = sb("et", [P, 2, F * P])
        prod = sb("prod", [P, TRING, FPT * P])
        prod_hi = sb("prod_hi", [P, TRING, FPT * P], F32R)
        prod_lo = sb("prod_lo", [P, LRING, FPT * P], F32R)
        hid = sb("hid", [P, HRING, BANK])
        stage = sb("stage", [P, 2, BANK])
        pair = sb("pair", [P, 2, HALVES, QPAD * FPC])
        back = sb("back", [P, HALVES, SKEW + F])
        mx = sb("mx", [P, 2, HALVES, F])
        mrow = sb("mrow", [P, HALVES, FX])
        zn = sb("zn", [P, 3, 2 * HALVES, F])
        rz = sb("rz", [P, HALVES, F])
        share = sb("share", [P, HALVES, F])
        inter = sb("inter", [P, G * HALVES])
        linear = sb("linear", [P, G * HALVES])
        logit = sb("logit", [P, 2, G * HALVES])
        prob = sb("prob", [P, G * HALVES])
        y_rows = sb("y_rows", [G * HALVES, P])
        ps = ctx.enter_context(nc.psum_tensor("ps", [P, 8, BANK], F32))
        Z, S, D, T = (0, 1, 2), (3, 4), (5, 6), 7

        w_zero = sem("w_zero")
        w_loaded = sem("w_loaded")
        w_ready = sem("w_ready")
        w1_rounded = sem("w1_rounded")
        id_ready = sem("id_ready")
        gate_done = sem("gate_done")
        idx_loaded = sem("idx_loaded")
        first_rows = [sem(f"first_rows{i}") for i in range(NET)]
        gathered = sem("gathered")
        lin_done = sem("lin_done")
        et_done = sem("et_done")
        et_copied = sem("et_copied")
        prod_ready = sem("prod_ready")
        hi_ready = sem("hi_ready")
        own_hi = sem("own_hi")
        lo_ready = sem("lo_ready")
        prod_used = sem("prod_used")
        z_done = sem("z_done")
        hid_ready = sem("hid_ready")
        block_done = sem("block_done")
        block_staged = sem("block_staged")
        sg_done = sem("sg_done")
        sg_copied = sem("sg_copied")
        tail = sem("tail")
        row_max = sem("row_max")
        slot_zero = sem("slot_zero")
        exp_done = sem("exp_done")
        logit_ready = sem("logit_ready")
        prob_ready = sem("prob_ready")
        y_turned = sem("y_turned")
        y_ready = sem("y_ready")
        stored = sem("stored")

        block = ctx.enter_context(nc.Block())

        def wait(eng, s, value):
            if not isinstance(value, int) or value > 0:
                eng.wait_ge(s, value)

        def over_groups(eng, body):
            body(0, True, False)
            with eng.Fori(1, G - 1) as g:
                body(g, False, False)
            body(G - 1, False, True)

        def parity(g):
            return g % 2 if isinstance(g, int) else g & 1

        def skewable(t):
            return t[:, :, 0:SKEW].rearrange("p h (d x) -> p h d x", x=2 * F)

        def skewed(t):
            return t[:, :, F - 1:F - 1 + NSK * (2 * F - 1)].rearrange("p h (d x) -> p h x d", x=2 * F - 1)[:, :, 0:F, :]

        STAGE_AT = {30: 0, 42: 1, 50: 2}
        STAGE_LAST_AT = 0
        TURN_AT = {40: (0, 0), 41: (0, 1), 45: (1, 0), 48: (1, 1), 51: (2, 0), 52: (2, 1)}
        TURN_LAST_AT = {2: 0, 7: 1}
        FIRST_ET_AT = {2: 6, 3: 7, 5: 8, 6: 9}
        ET_AT = {k: i for i, k in enumerate((26, 28, 29, 31, 32, 33, 34, 37, 44, 46))}
        LIN_AT = 37
        FIRST_LIN_AT = 6
        LOAD_AT, FIRST_LOAD_AT = 0, 7
        EXP_AT = {18: 1, 20: 0}
        assert NB == 4 and len(ET_AT) == NET and FIRST_LIN_AT < LIN_AT and max(FIRST_ET_AT) < FIRST_LOAD_AT < min(ET_AT)
        for at, n in STAGE_AT.items():
            assert SLOTS * (n + 1) <= at < SLOTS * (n + 2) - 1
            assert all(k < at for k, (m, _) in TURN_AT.items() if m < n) and all(k > at for k, (m, _) in TURN_AT.items() if m == n)

        def split_before(g, j):
            return g * (NT - len(whole)) + len([t for t in range(j) if t not in whole])

        def own_before(g, j):
            return g * len(own) + len([t for t in own if t < j])

        def pieces_before(g, j):
            return g * (2 * (NT - len(whole) - len(own))) + 2 * len([t for t in range(j) if t not in whole and t not in own])

        def rows_there(eng, n):
            if isinstance(n, int) and n == 0:
                for s in first_rows:
                    eng.wait_ge(s, 16 * FPC * HALVES)
            else:
                eng.wait_ge(gathered, n * (16 * FH))

        @block.sync
        def _(sp):
            sp.dma_start(idx[:], x_idx[0]).then_inc(idx_loaded, 16)
            sp.wait_ge(w_zero, 1)
            for h in range(HALVES):
                half = slice(K * h, K * (h + 1))
                sp.dma_start(w1_diag[half, half], W1).then_inc(w_loaded, 16)
                sp.dma_start(w2_col[half, :], W2).then_inc(w_loaded, 16)
                sp.dma_start(wf_col[half, :], Wf).then_inc(w_loaded, 16)
                sp.dma_start(b1_col[half, :], b1.rearrange("(a o) -> a o", o=1)).then_inc(w_loaded, 16)
            sp.dma_start(b2_col[:], b2.rearrange("(a o) -> a o", o=1).to_broadcast([P, 1])).then_inc(w_loaded, 16)
            sp.dma_start(bf_col[:], bf.rearrange("(a o) -> a o", o=1).to_broadcast([P, 1])).then_inc(w_loaded, 16)
            sp.wait_ge(y_ready, 1)
            sp.dma_start(out.rearrange("(c p) -> c p", p=P), y_rows[:]).then_inc(stored, 16)
            sp.wait_ge(stored, 16)

        @block.gpsimd
        def _(pool):
            nc.gpsimd.memset(gate[:], 0.0).then_inc(gate_done, 1)
            pool.wait_ge(gate_done, 1)
            nc.gpsimd.memset(w1_diag[:], 0.0).then_inc(w_zero, 1)


            def gather(g, first=False):
                pool.wait_ge(idx_loaded, g * 16 + 16)
                pool.wait_ge(gate_done, g + 1)
                nc.gpsimd.tensor_tensor(gate[:, 1:2], gate[:, 0:1], gate[:, 0:1], ALU.add).then_inc(gate_done, 1)
                for r in range(FH):
                    nc.gpsimd.indirect_dma_start(
                        out=raw[:, r // HALVES, ROW * (r % HALVES):ROW * (r % HALVES + 1)], out_offset=None,
                        in_=(lin_first, lin_last)[r % HALVES],
                        in_offset=bass.IndirectOffsetOnAxis(ap=idx[:, r:r + 1], axis=0)).then_inc(
                            first_rows[r // (FPC * HALVES)] if first else gathered, 16)

            nc.gpsimd.memset(ident[:], 0.0).then_inc(w_zero, 1)
            pool.wait_ge(w_zero, 2)
            nc.gpsimd.affine_select(out=ident[:], in_=ident[:], compare_op=ALU.not_equal, fill=1.0, base=0,
                                    pattern=[[-1, P]], channel_multiplier=1).then_inc(id_ready, 1)
            gather(0, first=True)
            with pool.Fori(1, G) as g:
                gather(g)

        @block.tensor
        def _(pe):
            def turn_embeddings(n, i):
                if isinstance(n, int) and n == 0:
                    pe.wait_ge(first_rows[i], 16 * FPC * HALVES)
                else:
                    if i == 0:
                        pe.wait_ge(gathered, n * (16 * FH))
                    before = len([k for k in TURN_AT if k <= min(k for k in ET_AT if ET_AT[k] == i)])
                    wait(pe, sg_copied, (n - 1) * (4 * NB) + 2 * before)
                wait(pe, et_copied, n * NET + i)
                for j in range(FPC):
                    f = FPC * i + j
                    mm = nc.tensor.transpose(ps[:, T, P * j:P * (j + 1)], raw[:, f, 1:1 + HALVES * K], ident[:])
                mm.then_inc(et_done, 1)

            def hidden(g, k):
                for q in range(STEP * k, min(STEP * k + STEP, NQ)):
                    j, at = q // CPT, slice(BANK * (q % CPT), BANK * (q % CPT + 1))
                    if q % CPT == 0 and j not in whole:
                        pe.wait_ge(lo_ready, split_before(g, j) + 1)
                    wait(pe, hid_ready, g * NQ + (q - 2))
                    z = ps[:, Z[q % 3], :]
                    if j in whole:
                        mm = nc.tensor.matmul(z, w1_diag[:], prod[:, j % TRING, at], start=True, stop=True)
                    else:
                        hi, lo = prod_hi[:, j % TRING, at], prod_lo[:, j % LRING, at]
                        nc.tensor.matmul(z, w1_hi[:], hi, start=True, stop=False)
                        nc.tensor.matmul(z, w1_hi[:], lo, start=False, stop=False)
                        mm = nc.tensor.matmul(z, w1_lo[:], hi, start=False, stop=True)
                    mm.then_inc(z_done, 1)

            def dots(g, k):
                n, t = k // SLOTS, k % SLOTS
                if t == 0:
                    wait(pe, block_staged, g * (2 * NB) + 2 * (n - 1))
                for c, q in enumerate(range(STEP * k, min(STEP * k + STEP, NQ))):
                    if q % CPT == 0:
                        pe.wait_ge(prod_ready, g * NT + (q // CPT + 1))
                    mm = nc.tensor.matmul(ps[32 * c:32 * c + 32, D[n % 2], :], wf_slot[:, 32 * t:32 * t + 32],
                                          prod[:, (q // CPT) % TRING, BANK * (q % CPT):BANK * (q % CPT + 1)],
                                          start=(t == 0), stop=(t == slots_of(n, c) - 1))
                    if q % CPT == CPT - 1:
                        mm.then_inc(prod_used, 1)

            def scores(g, k):
                n, t = k // SLOTS, k % SLOTS
                qs = range(STEP * k, min(STEP * k + STEP, NQ))
                pe.wait_ge(hid_ready, g * NQ + (qs[-1] + 1))
                for c, q in enumerate(qs):
                    mm = nc.tensor.matmul(ps[32 * c:32 * c + 32, S[n % 2], :], w2_slot[:, 32 * t:32 * t + 32],
                                          hid[:, q % HRING, :], start=(t == 0), stop=(t == slots_of(n, c) - 1))
                if t == SLOTS - 1 or k == NS - 1:
                    mm.then_inc(block_done, 1)

            def slots_of(n, c):
                return len([k for k in range(SLOTS * n, min(SLOTS * n + SLOTS, NS)) if STEP * k + c < NQ])

            def turn_block(g, n, which, after_et):
                pe.wait_ge(block_staged, g * (2 * NB) + (2 * n + which + 1))
                wait(pe, sg_copied, g * (4 * NB) + (4 * n + 2 * which))
                pe.wait_ge(et_copied, after_et)
                for j in range(FPC):
                    mm = nc.tensor.transpose(ps[:, T, P * j:P * (j + 1)], stage[:, which, P * j:P * (j + 1)], ident[:])
                mm.then_inc(sg_done, 1)

            def body(g, first, last):
                dots(g, 0)
                for k in range(NS):
                    hidden(g, k)
                    if k + 1 < NS - 1:
                        dots(g, k + 1)
                    if k > 0:
                        scores(g, k - 1)
                    elif not first:
                        scores(g - 1, NS - 1)
                    if first and k in FIRST_ET_AT:
                        turn_embeddings(0, FIRST_ET_AT[k])
                    if not first and k in TURN_LAST_AT:
                        turn_block(g - 1, NB - 1, TURN_LAST_AT[k], g * NET + NET)
                    if k in TURN_AT:
                        n, which = TURN_AT[k]
                        later = 0 if last else len([e for e in ET_AT if e < k])
                        turn_block(g, n, which, g * NET + (NET + later))
                    if not last and k in ET_AT:
                        turn_embeddings(g + 1, ET_AT[k])
                dots(g, NS - 1)

            pe.wait_ge(id_ready, 1)
            for i in range(NET - len(FIRST_ET_AT)):
                turn_embeddings(0, i)
            pe.wait_ge(w_loaded, 16 * (4 * HALVES + 2))
            pe.wait_ge(w_ready, 2 * HALVES + 1)
            over_groups(pe, body)
            scores(G - 1, NS - 1)
            for which in range(2):
                turn_block(G - 1, NB - 1, which, G * NET)
            pe.wait_ge(prob_ready, 1)
            nc.tensor.transpose(ps[0:G * HALVES, T, 0:P], prob[:], ident[:]).then_inc(y_turned, 1)

        @block.scalar
        def _(act):
            def copy_embeddings(n, i):
                act.wait_ge(et_done, n * NET + (i + 1))
                home = et[:, bass.ds(parity(n), 1), :].rearrange("p a x -> p (a x)")
                nc.scalar.copy(home[:, BANK * i:BANK * (i + 1)], ps[:, T, :]).then_inc(et_copied, 1)

            def round_behind(j, piece):
                if j in whole or j in own:
                    return None
                return CPT * (j - 2) + (SHIFTED_AT if j in shifted else ROUND_AT)[piece]

            def round_piece(g, j, piece):
                if piece == 0:
                    act.wait_ge(prod_ready, g * NT + (j + 1))
                    wait(act, z_done, g * NQ + CPT * (j - TRING + 1))
                at = slice(0, BANK * ROUND_CUT) if piece == 0 else slice(BANK * ROUND_CUT, BANK * CPT)
                nc.scalar.copy(prod_hi[:, j % TRING, at], prod[:, j % TRING, at]).then_inc(hi_ready, 1)

            def stage_block(g, n):
                act.wait_ge(block_done, g * NB + (n + 1))
                wait(act, sg_done, g * (2 * NB) + 2 * n)
                nc.scalar.copy(stage[:, 0, :], ps[:, S[n % 2], :]).then_inc(block_staged, 1)
                nc.scalar.copy(stage[:, 1, :], ps[:, D[n % 2], :]).then_inc(block_staged, 1)

            def unpack_block(g, n, which):
                slots = min(SLOTS, NS - SLOTS * n)
                act.wait_ge(sg_done, g * (2 * NB) + (2 * n + which + 1))
                if n == 0 and which == 0:
                    wait(act, tail, g * NTAIL)
                src = ps[:, T, :].rearrange("p (i c h t) -> p i c h t", i=FPC, c=STEP, h=HALVES)
                for h in range(HALVES):
                    a = SLOTS * STEP * FPC * n
                    to = pair[:, which, h, a:a + slots * STEP * FPC].rearrange("p (t c i) -> p i c t", c=STEP, i=FPC)
                    if which == 0:
                        nc.scalar.activation(to, src[:, :, :, h, 0:slots], ACT.Identity,
                                             bias=b2_col[:, 0:1]).then_inc(sg_copied, 1)
                    else:
                        nc.scalar.copy(to, src[:, :, :, h, 0:slots]).then_inc(sg_copied, 1)

            def exponentials(g, which):
                if which == 1:
                    act.wait_ge(tail, g * NTAIL + 6)
                    v = skewable(back)[:, :, :, 0:F]
                else:
                    act.wait_ge(tail, g * NTAIL + 7)
                    v = pair[:, 0, :, 0:ND * F]
                nc.scalar.activation(v, v, ACT.Exp).then_inc(exp_done, 1)

            def load_indices(n):
                act.wait_ge(lin_done, n * 1)
                nc.scalar.dma_start(idx[:], x_idx[bass.ds(n, 1)].rearrange("a p f -> (a p) f")).then_inc(idx_loaded, 16)

            def body(g, first, last):
                for k in range(NS):
                    if not last and k == (FIRST_LOAD_AT if first else LOAD_AT):
                        load_indices(g + 1)
                    for q in range(STEP * k, min(STEP * k + STEP, NQ)):
                        act.wait_ge(z_done, g * NQ + (q + 1))
                        nc.scalar.activation(hid[:, q % HRING, :], ps[:, Z[q % 3], :], ACT.Relu,
                                             bias=b1_col[:, 0:1]).then_inc(hid_ready, 1)
                        for j in range(q // CPT + 1, q // CPT + 3):
                            for piece in range(2):
                                if round_behind(j % NT, piece) == q - CPT * (j // NT * NT):
                                    if j < NT:
                                        round_piece(g, j, piece)
                                    elif not last:
                                        round_piece(g + 1, j - NT, piece)
                    if k in STAGE_AT:
                        stage_block(g, STAGE_AT[k])
                    if k in TURN_AT:
                        unpack_block(g, *TURN_AT[k])
                    if first and k in FIRST_ET_AT:
                        copy_embeddings(0, FIRST_ET_AT[k])
                    if not first:
                        if k == STAGE_LAST_AT:
                            stage_block(g - 1, NB - 1)
                        if k in TURN_LAST_AT:
                            unpack_block(g - 1, NB - 1, TURN_LAST_AT[k])
                        if k in EXP_AT:
                            exponentials(g - 1, EXP_AT[k])
                    if not last and k in ET_AT:
                        copy_embeddings(g + 1, ET_AT[k])

            act.wait_ge(w_loaded, 16 * (4 * HALVES + 2))
            nc.scalar.copy(w1_hi[:], w1_diag[:]).then_inc(w1_rounded, 1)
            for i in range(NET - len(FIRST_ET_AT)):
                copy_embeddings(0, i)
            for j in range(2):
                for piece in range(2):
                    if (round_behind(j, piece) or 0) < 0:
                        round_piece(0, j, piece)
            over_groups(act, body)
            stage_block(G - 1, NB - 1)
            for which in range(2):
                unpack_block(G - 1, NB - 1, which)
            exponentials(G - 1, 1)
            exponentials(G - 1, 0)
            act.wait_ge(logit_ready, 1)
            nc.scalar.activation(prob[:], logit[:, 1, :], ACT.Sigmoid, bias=bf_col[:, 0:1]).then_inc(prob_ready, 1)

        @block.vector
        def _(dve):
            def product(g, j):
                side, d = divmod(j, ND)
                i0 = side * FPT
                if isinstance(g, int) and g == 0:
                    dve.wait_ge(et_copied, min(NET, -(-(i0 + FPT + d) // FPC)))
                elif j == 0:
                    dve.wait_ge(et_copied, g * NET + NET)
                wait(dve, prod_used, g * NT + (j - TRING + 1))
                if (j - TRING) % NT in whole:
                    wait(dve, z_done, g * NQ + CPT * (j - TRING + 1))
                home = et[:, bass.ds(parity(g), 1), :].rearrange("p a x -> p (a x)")
                straight = min(FPT, F - i0 - d)
                for a, b, to in ((0, straight, i0 + d), (straight, FPT, 0)):
                    if a < b:
                        ins = nc.vector.tensor_tensor(prod[:, j % TRING, P * a:P * b], home[:, P * (i0 + a):P * (i0 + b)],
                                                      home[:, P * to:P * (to + b - a)], ALU.mult)
                ins.then_inc(prod_ready, 1)

            def round_tile(g, j):
                dve.wait_ge(prod_ready, g * NT + (j + 1))
                wait(dve, z_done, g * NQ + CPT * (j - TRING + 1))
                nc.vector.tensor_copy(prod_hi[:, j % TRING, :], prod[:, j % TRING, :]).then_inc(own_hi, 1)

            def rest_of_tile(g, j):
                if j in own:
                    dve.wait_ge(own_hi, own_before(g, j) + 1)
                else:
                    dve.wait_ge(hi_ready, pieces_before(g, j) + 2)
                wait(dve, z_done, g * NQ + CPT * (j - LRING + 1))
                dve.wait_ge(prod_ready, g * NT + (j + 1))
                nc.vector.tensor_tensor(prod_lo[:, j % LRING, :], prod[:, j % TRING, :],
                                        prod_hi[:, j % TRING, :].bitcast(F32), ALU.subtract).then_inc(lo_ready, 1)

            def linear_part(n):
                rows_there(dve, n)
                nc.vector.tensor_reduce(linear[:, bass.ds(n * HALVES, HALVES)],
                                        raw[:, :, 0:HALVES * ROW:HALVES * ROW - 1].rearrange("p f h -> p h f"), AX_X,
                                        ALU.add).then_inc(lin_done, 1)

            def diagonals(which, side, a, b):
                at = ND * FPT * side
                return pair[:, which, :, at + FPT * a:at + FPT * b].rearrange("p h (d i) -> p h d i", i=FPT)

            def on_side(view, side):
                return view[..., FPT * side:FPT * (side + 1)]

            def softmax_step(g, s):
                def after(step):
                    dve.wait_ge(tail, g * NTAIL + (step + 1))

                once, again = skewable(back)[:, :, :, 0:F], skewable(back)[:, :, :, F:2 * F]
                sides = range(SIDES)
                if s == 0:
                    dve.wait_ge(sg_copied, g * (NB * 4) + NB * 4)
                    for side in sides:
                        ins = nc.vector.tensor_copy(on_side(once, side), diagonals(0, side, 1, NSK + 1))
                elif s == 1:
                    for side in sides:
                        ins = nc.vector.tensor_copy(on_side(again, side), diagonals(0, side, 1, NSK + 1))
                elif s == 2:
                    for side in sides:
                        ins = nc.vector.tensor_reduce(on_side(mx[:, 0], side),
                                                      diagonals(0, side, 0, ND).rearrange("p h d i -> p h i d"), AX_X,
                                                      ALU.max)
                elif s == 3:
                    after(1)
                    ins = nc.vector.tensor_reduce(mx[:, 1], skewed(back), AX_X, ALU.max)
                elif s == 4:
                    after(3)
                    nc.vector.tensor_tensor(mrow[:, :, 0:F], mx[:, 0], mx[:, 1], ALU.max).then_inc(row_max, 1)
                    dve.wait_ge(row_max, g + 1)
                    ins = nc.vector.tensor_copy(mrow[:, :, F:FX], mrow[:, :, 0:FX - F])
                elif s == 5:
                    after(4)
                    for side in sides:
                        row_of = bass.AP(tensor=mrow[:].tensor, offset=FPT * side + 1,
                                         ap=[[HALVES * FX, P], [FX, HALVES], [1, NSK], [1, FPT]])
                        ins = nc.vector.tensor_tensor(on_side(once, side), diagonals(0, side, 1, NSK + 1), row_of,
                                                      ALU.subtract)
                elif s == 6:
                    after(5)
                    for side in sides:
                        own_row = on_side(mrow[:, :, 0:F], side).unsqueeze(2).to_broadcast([P, HALVES, ND, FPT])
                        ins = nc.vector.tensor_tensor(diagonals(0, side, 0, ND), diagonals(0, side, 0, ND), own_row,
                                                      ALU.subtract)
                elif s == 7:
                    dve.wait_ge(exp_done, g * 2 + 1)
                    ins = nc.vector.tensor_copy(again, once)
                elif s == 8:
                    after(7)
                    ins = nc.vector.tensor_reduce(zn[:, 1, 0:HALVES], skewed(back), AX_X, ALU.add)
                elif s == 9:
                    after(8)
                    for side in sides:
                        ins = nc.vector.tensor_tensor(on_side(once, side), on_side(once, side),
                                                      diagonals(1, side, 1, NSK + 1), ALU.mult)
                elif s == 10:
                    after(9)
                    ins = nc.vector.tensor_copy(again, once)
                elif s == 11:
                    after(10)
                    ins = nc.vector.tensor_reduce(zn[:, 1, HALVES:2 * HALVES], skewed(back), AX_X, ALU.add)
                elif s == 12:
                    dve.wait_ge(exp_done, g * 2 + 2)
                    ins = nc.vector.tensor_tensor(pair[:, 1, :, 0:ND * F], pair[:, 0, :, 0:ND * F],
                                                  pair[:, 1, :, 0:ND * F], ALU.mult)
                elif s == 13:
                    after(12)
                    for side in sides:
                        v = pair[:, :, :, ND * FPT * side:ND * FPT * (side + 1)].rearrange("p w h x -> p (w h) x")
                        ins = nc.vector.tensor_reduce(on_side(zn[:, 0], side), v.rearrange("p w (d i) -> p w i d", i=FPT),
                                                      AX_X, ALU.add)
                elif s == 14:
                    after(13)
                    ins = nc.vector.tensor_tensor(zn[:, 2], zn[:, 0], zn[:, 1], ALU.add)
                elif s == 15:
                    after(14)
                    ins = nc.vector.reciprocal(rz[:], zn[:, 2, 0:HALVES])
                elif s == 16:
                    after(15)
                    ins = nc.vector.tensor_tensor(share[:], zn[:, 2, HALVES:2 * HALVES], rz[:], ALU.mult)
                elif s == 17:
                    after(16)
                    ins = nc.vector.tensor_reduce(inter[:, bass.ds(g * HALVES, HALVES)], share[:], AX_X, ALU.add)
                ins.then_inc(tail, 1)

            def body(g, first, last):
                for j in range(NT):
                    product(g, j)
                    if j in own:
                        round_tile(g, j)
                    if (j - 1) % NT not in whole:
                        if j > 0:
                            rest_of_tile(g, j - 1)
                        elif not first:
                            rest_of_tile(g - 1, NT - 1)
                    if not first:
                        for s in SOFTMAX_AT.get(j, ()):
                            softmax_step(g - 1, s)
                    if first and j == FIRST_LIN_AT:
                        linear_part(0)
                    if not last and j == LIN_AT:
                        linear_part(g + 1)

            dve.wait_ge(w1_rounded, 1)
            nc.vector.tensor_tensor(w1_lo[:], w1_diag[:], w1_hi[:].bitcast(F32), ALU.subtract).then_inc(w_ready, 1)
            nc.vector.memset(w2_slot[:], 0.0).then_inc(slot_zero, 1)
            nc.vector.memset(wf_slot[:], 0.0).then_inc(slot_zero, 1)
            dve.wait_ge(slot_zero, 2)
            dve.wait_ge(w_loaded, 16 * (4 * HALVES + 2))
            for slot, col in ((w2_slot, w2_col), (wf_slot, wf_col)):
                for h in range(HALVES):
                    half = slice(K * h, K * (h + 1))
                    to = bass.AP(tensor=slot[:].tensor, offset=K * h * SLOTS * 32 + SLOTS * h,
                                 ap=[[SLOTS * 32, K], [33, SLOTS]])
                    nc.vector.tensor_copy(to, col[half, 0:1].to_broadcast([K, SLOTS])).then_inc(w_ready, 1)
            over_groups(dve, body)
            if NT - 1 not in whole:
                rest_of_tile(G - 1, NT - 1)
            for s in range(NTAIL):
                softmax_step(G - 1, s)
            dve.wait_ge(tail, G * NTAIL)
            dve.wait_ge(lin_done, G)
            nc.vector.tensor_tensor(logit[:, 1, :], inter[:], linear[:], ALU.add).then_inc(logit_ready, 1)
            dve.wait_ge(y_turned, 1)
            nc.vector.tensor_copy(y_rows[:], ps[0:G * HALVES, T, 0:P]).then_inc(y_ready, 1)


def kernel(**inputs):
    import numpy as np
    import concourse.bacc as bacc
    from concourse.bass_utils import run_bass_kernel_spmd

    x = np.asarray(inputs["r_x"])
    batch, fields = x.shape
    groups = batch // (HALVES * P)
    x = x.reshape(groups, HALVES, P, fields).transpose(0, 2, 3, 1).reshape(groups, P, fields * HALVES)
    V, lin = inputs["L0_rec_V_table"], inputs["L0_rec_lin_table"]
    arrays = {"x_idx": x, "lin_first": np.concatenate([lin, V], axis=1), "lin_last": np.concatenate([V, lin], axis=1)}
    for name in ("W1", "b1", "W2", "b2", "Wf", "bf"):
        arrays[name] = inputs["L0_rec_" + name]
    arrays = {n: np.ascontiguousarray(a) for n, a in arrays.items()}

    nc = bacc.Bacc("TRN2", target_bir_lowering=False, num_devices=1)
    args = [nc.dram_tensor(n, a.shape, mybir.dt.from_np(a.dtype), kind="ExternalInput").ap() for n, a in arrays.items()]
    args.append(nc.dram_tensor("y", (batch,), F32, kind="ExternalOutput").ap())
    attentional_fm(nc, *args)
    r = run_bass_kernel_spmd(nc, [arrays], core_ids=[0])
    return r.results[0]["y"]
```
